# Optimizing a Trainium2 kernel written in Bass

```python
import numpy as np
import jax
import jax.numpy as jnp

def _softmax(x, axis=-1):
    return jax.nn.softmax(x, axis=axis)
def _gelu(x):
    return jax.nn.gelu(x, approximate=True)
def _silu(x):
    return jax.nn.silu(x)
def _sigmoid(x):
    return jax.nn.sigmoid(x)
def _layernorm(x, axis=-1, eps=1e-5):
    m = jnp.mean(x, axis=axis, keepdims=True)
    v = jnp.var(x, axis=axis, keepdims=True)
    return (x - m) / jnp.sqrt(v + eps)
def _scatter_add(tgt, idx, src, axis=0):
    return tgt.at[idx].add(src)
def _segment_sum(src, seg, n):
    return jax.ops.segment_sum(src, seg, n)

kernel_name = 'mk_adj_resnorm_d2_adj_128_bf9c23'

def setup_inputs(seed: int = 0):
    np.random.seed(seed)
    _w = jnp.asarray
    def _rec_inputs():
        import jax
        import jax.numpy as jnp
        _gk = jax.random.key(seed)
        x = -0.000929 + 1 * jax.random.normal(jax.random.fold_in(_gk, 1), (8192, 128), jnp.float32)
        _a = jax.random.bernoulli(jax.random.fold_in(_gk, 2), 0.000976562, (8192, 8192))
        _a = jnp.logical_or(_a, jnp.eye(8192, dtype=bool))
        _af = _a.astype(jnp.float32)
        _af = _af * jax.random.uniform(jax.random.fold_in(_gk, 3), (8192, 8192), jnp.float32, 0.05, 1)
        adj = _af
        return x, adj
    x, adj = _rec_inputs()
    def _L0_gnn_setup():
        import jax, jax.numpy as jnp
        import numpy as np
        N = 8192
        F_IN = 128
        F_OUT = 128
        key = jax.random.key(seed)
        k1, k2, k3, k4, k5 = jax.random.split(key, 5)
        x = jax.random.normal(k1, (N, F_IN), dtype=jnp.float32)
        adj = jax.random.uniform(k2, (N, N), dtype=jnp.float32)
        kernel = jax.random.normal(k3, (F_IN, F_OUT), dtype=jnp.float32) * 0.05
        bias = jax.random.normal(k4, (F_OUT,), dtype=jnp.float32) * 0.05
        beta = jax.random.uniform(k5, (N,), dtype=jnp.float32)
        return {'x': x, 'adj': adj, 'kernel': kernel, 'bias': bias, 'beta': beta}
    _L0_gnn_all = _L0_gnn_setup()
    _L0_gnn_in = {k: v for k, v in _L0_gnn_all.items() if k in ('kernel', 'bias', 'beta', )}
    del _L0_gnn_all

    def _L1_gnn_setup():
        import jax, jax.numpy as jnp
        import numpy as np
        V0, V1, C = (64, 128, 128)
        V = V0 * V1
        key = jax.random.key(seed)
        ks = jax.random.split(key, 8)
        x = jax.random.normal(ks[0], (V, C), dtype=jnp.float32)
        edge_index = jax.random.randint(ks[1], (2, 100), 0, V)
        L = jnp.zeros((2, 2), dtype=jnp.float32)
        mass = jax.random.uniform(ks[2], (V,), dtype=jnp.float32) + 0.5
        evals0 = jax.random.uniform(ks[3], (V0,), dtype=jnp.float32) * 2.0
        evals1 = jax.random.uniform(ks[4], (V1,), dtype=jnp.float32) * 2.0
        evecs = jax.random.normal(ks[5], (V, V), dtype=jnp.float32) / np.float32(np.sqrt(V))
        diffusion_time = jax.random.uniform(ks[6], (2, C), dtype=jnp.float32)
        return {'x': x, 'edge_index': edge_index, 'L': L, 'mass': mass, 'evals0': evals0, 'evals1': evals1, 'evecs': evecs, 'diffusion_time': diffusion_time}
    _L1_gnn_all = _L1_gnn_setup()
    _L1_gnn_in = {k: v for k, v in _L1_gnn_all.items() if k in ('edge_index', 'L', 'mass', 'evals0', 'evals1', 'diffusion_time', )}
    del _L1_gnn_all

    return {
        "x": x,
        "adj": adj,
        "L0_gnn_kernel": _L0_gnn_in["kernel"],
        "L0_gnn_bias": _L0_gnn_in["bias"],
        "L0_gnn_beta": _L0_gnn_in["beta"],
        "L1_gnn_edge_index": _L1_gnn_in["edge_index"],
        "L1_gnn_L": _L1_gnn_in["L"],
        "L1_gnn_mass": _L1_gnn_in["mass"],
        "L1_gnn_evals0": _L1_gnn_in["evals0"],
        "L1_gnn_evals1": _L1_gnn_in["evals1"],
        "L1_gnn_diffusion_time": _L1_gnn_in["diffusion_time"],
    }

def reference(x, adj, L0_gnn_kernel, L0_gnn_bias, L0_gnn_beta, L1_gnn_edge_index, L1_gnn_L, L1_gnn_mass, L1_gnn_evals0, L1_gnn_evals1, L1_gnn_diffusion_time):
    import jax
    import jax.numpy as jnp
    def _L0_gnn_ref(x, adj, kernel, bias, beta):
        import jax, jax.numpy as jnp
        import numpy as np
        N = 8192
        F_IN = 128
        F_OUT = 128
        inv_deg = 1.0 / (jnp.sum(adj, axis=1) + beta)
        agg = adj @ x + beta[:, None] * x
        out = inv_deg[:, None] * agg @ kernel + bias
        return out

    def _L1_gnn_ref(x, edge_index, L, mass, evals0, evals1, evecs, diffusion_time):
        import jax, jax.numpy as jnp
        import numpy as np
        V0, V1, C = (64, 128, 128)
        V = V0 * V1
        x_spec = evecs.T @ (x * mass[:, None])
        e0 = jnp.exp(-evals0[:, None] * diffusion_time[0][None, :])
        e1 = jnp.exp(-evals1[:, None] * diffusion_time[1][None, :])
        diffusion_coefs = (e0[:, None, :] * e1[None, :, :]).reshape(V0 * V1, C)
        x_diffuse = evecs @ (diffusion_coefs * x_spec)
        return x_diffuse

    x = _layernorm(x + _L0_gnn_ref(x, adj, L0_gnn_kernel, L0_gnn_bias, L0_gnn_beta), axis=-1)
    x = _layernorm(x + _L1_gnn_ref(x, L1_gnn_edge_index, L1_gnn_L, L1_gnn_mass, L1_gnn_evals0, L1_gnn_evals1, adj, L1_gnn_diffusion_time), axis=-1)
    return x


_drawn_inputs = setup_inputs


def setup_inputs(seed=0):
    import zlib

    import numpy as np

    out = dict(_drawn_inputs(seed))
    spreads = {'L1_gnn_L': (0.0, 0.1)}
    factors = {}
    for name, (base, spread) in spreads.items():
        noise = np.random.default_rng([zlib.crc32(name.encode()), seed]).standard_normal(out[name].shape)
        drawn = base * np.exp(spread * noise) if base else spread * noise
        out[name] = jnp.asarray(drawn.astype(out[name].dtype))
    for name, factor in factors.items():
        out[name] = (out[name] * factor).astype(out[name].dtype)
    return out
```

```python
from contextlib import ExitStack

import concourse.bass as bass
from concourse import mybir

F32 = mybir.dt.float32
F32R = mybir.dt.float32r
ALU = mybir.AluOpType
ACT = mybir.ActivationFunctionType

P = 128
N = 8192
F = 128
W = 512
TILES = N // P
BLOCKS = N // W
SUB = W // P
CHUNK = SUB * W
HALF = CHUNK // 2
RAW = 8
SPLIT = 4
LEAD = 3
EPS = 1e-5

BODY = [step for k in range(BLOCKS - LEAD) for step in (("A", k), ("T", k + LEAD))]
BODY += [("A", c) for c in range(BLOCKS - LEAD, BLOCKS)]
LAST_BODY = list(BODY)
BODY += [("T", g) for g in range(LEAD)]
HEAD = BLOCKS + LEAD
PASSES = BLOCKS - 2
LAST = HEAD + PASSES * len(BODY)
TAIL = LAST + len(LAST_BODY)
FINAL = TAIL + BLOCKS
assert len(BODY) % RAW == 0 and FINAL % RAW == 0 and FINAL == 2 * BLOCKS * BLOCKS


def build(nc, adj_t, adj_n, x_tiles, x_blocks, beta_mass, gnn_kernel, bias, evals0, evals1, times, x1_store, out):
    with ExitStack() as ctx:
        def sb(name, shape, dt=F32):
            return ctx.enter_context(nc.sbuf_tensor(name, shape, dt))

        def pb(name, shape):
            return ctx.enter_context(nc.psum_tensor(name, shape, F32))

        def sem(name):
            return ctx.enter_context(nc.semaphore(name))

        raw = sb("raw", [P, RAW, CHUNK])
        hi = sb("hi", [P, SPLIT, HALF], F32R)
        lo = sb("lo", [P, SPLIT, HALF], F32R)
        w_hi = sb("w_hi", [P, TILES * F], F32R)
        w_lo = sb("w_lo", [P, TILES * F], F32R)
        spec = sb("spec", [P, N])
        y_hi = sb("y_hi", [P, W], F32R)
        y_lo = sb("y_lo", [P, W], F32R)
        xi = sb("xi", [P, W])
        work = sb("work", [P, W])
        rows = sb("rows", [P, W])
        rows_end = sb("rows_end", [P, W])
        k_sb = sb("k_sb", [P, F])
        bias_sb = sb("bias_sb", [P, F])
        ident = sb("ident", [P, P])
        ones = sb("ones", [P, 1])
        e0 = sb("e0", [P, TILES])
        e1 = sb("e1", [P, P])
        t_sb = sb("t_sb", [P, 2])
        bm = sb("bm", [P, 2 * SUB])
        deg = sb("deg", [P, SUB])
        inv = sb("inv", [P, SUB])
        stats = sb("stats", [P, SUB, 6])
        mean = sb("mean", [P, SUB])
        gap = sb("gap", [P, SUB])
        var = sb("var", [P, SUB])
        root = sb("root", [P, SUB])
        quot = sb("quot", [P, SUB])
        rstd = sb("rstd", [P, SUB])
        res_t = spec[:, 0:2 * W].rearrange("p (b w) -> p b w", b=2)
        x1_in = spec[:, 2 * W:4 * W].rearrange("p (b w) -> p b w", b=2)
        fin = spec[:, 4 * W:6 * W].rearrange("p (b w) -> p b w", b=2)

        acc = pb("acc", [P, 2, W])
        part = pb("part", [P, 2, W])
        turned = pb("turned", [P, 2, W])
        kout = pb("kout", [P, W])
        degp = pb("degp", [P, W])

        s_raw = [sem(f"s_raw{i}") for i in range(RAW)]
        s_hi = sem("s_hi")
        s_lo = sem("s_lo")
        s_half = sem("s_half")
        s_rows = sem("s_rows")
        s_x = [sem(f"s_quarter{i}") for i in range(4)]
        s_whi = sem("s_whi")
        s_wlo = sem("s_wlo")
        s_zero = sem("s_zero")
        s_const = sem("s_const")
        s_ones = sem("s_ones")
        s_ident = sem("s_ident")
        s_negt = sem("s_negt")
        s_exp = sem("s_exp")
        s_xi = sem("s_xi")
        s_diag = sem("s_diag")
        s_agg = sem("s_agg")
        s_aggc = sem("s_aggc")
        s_kout = sem("s_kout")
        s_dve = sem("s_dve")
        s_var = sem("s_var")
        s_root = sem("s_root")
        s_y = sem("s_y")
        s_x1 = sem("s_x1")
        s_added = sem("s_added")
        s_coef = sem("s_coef")
        s_zt = sem("s_zt")
        s_zhi = sem("s_zhi")
        s_zlo = sem("s_zlo")
        s_res = sem("s_res")
        s_rt = sem("s_rt")
        s_x1in = [sem("s_x1in0"), sem("s_x1in1")]
        s_sum = sem("s_sum")
        s_fin = sem("s_fin")
        s_out = sem("s_out")

        CONSTS = 5
        CHAIN = 14
        CHAIN_END = 9
        TURN_AT, SUM_AT, ROOT_AT, OUT_AT = 3, 6, 8, 11
        Z_TURN, Z_SPLIT = 3, 6
        out_blocks = out.rearrange("(b k p) f -> b p k f", k=SUB, p=P)

        block = ctx.enter_context(nc.Block())

        L = len(BODY)

        def landed(eng, q, m):
            eng.wait_ge(s_raw[q % RAW], m * (16 * (L // RAW)) + 16 * (q // RAW + 1))

        @block.sync
        def _(sp):
            def load(src, index, q, m, tiles_before):
                if tiles_before is not None:
                    sp.wait_ge(s_rows, m * (SUB * BLOCKS) + SUB * tiles_before)
                elif not (isinstance(m, int) and q + L * m < RAW):
                    sp.wait_ge(s_lo, m * (2 * L) + 2 * (q - RAW) + 2)
                sp.dma_start(raw[:, q % RAW, :], src[bass.ds(index, 1), :, :].rearrange("a p n -> p (a n)"))\
                  .then_inc(s_raw[q % RAW], 16)

            for g in range(HEAD):
                if g < 4:
                    quarter = slice(g * N // 4, (g + 1) * N // 4)
                    sp.dma_start(spec[:, quarter], x_tiles[:, quarter]).then_inc(s_x[g], 16)
                load(adj_t, g, g, 0, g - RAW + 1 if g >= RAW else None)

            def seen(order, q):
                if q < 0:
                    count = LEAD + sum(k == "T" for k, _ in BODY[:q + L + 1])
                    return count if BODY[q + L][0] == "T" else None
                return HEAD + sum(k == "T" for k, _ in order[:q + 1]) if order[q][0] == "T" else None

            def one_pass(order, q0, m):
                for q, (kind, g) in enumerate(order):
                    before = seen(order, q - RAW)
                    if isinstance(m, int) and m == 0 and q < RAW:
                        before = HEAD + q - RAW + 1
                    if kind == "A":
                        load(adj_n, m * BLOCKS + g, q0 + q, m, before)
                    else:
                        load(adj_t, m * BLOCKS + (g + BLOCKS if g >= LEAD else g + 2 * BLOCKS), q0 + q, m, before)

            one_pass(BODY, HEAD, 0)
            with sp.Fori(1, PASSES) as m:
                one_pass(BODY, HEAD, m)
            one_pass(LAST_BODY, HEAD, PASSES)
            for c in range(BLOCKS):
                before = seen(LAST_BODY, len(LAST_BODY) + c - RAW) if c < RAW else None
                load(adj_n, (BLOCKS - 1) * BLOCKS + c, TAIL + c, 0, before and PASSES * BLOCKS + before)

            def final(q0, m, first):
                for g in range(BLOCKS):
                    load(adj_t, m * (2 * BLOCKS) + first + g, q0 + g, m, None)

            final(FINAL, 0, 0)
            with sp.Fori(0, (BLOCKS - 2) // 2) as m:
                final(FINAL + BLOCKS, m, BLOCKS)
                final(FINAL + 2 * BLOCKS, m, 2 * BLOCKS)
            final(FINAL + (BLOCKS - 1) * BLOCKS, 0, (BLOCKS - 1) * BLOCKS)
            sp.wait_ge(s_out, 16 * BLOCKS)
            sp.wait_ge(s_x1, 16 * BLOCKS)

        @block.gpsimd
        def _(pool):
            nc.gpsimd.memset(ones[:, :], 1.0).then_inc(s_ones, 1)
            nc.gpsimd.memset(ident[:, :], 0.0).then_inc(s_ident, 1)
            pool.wait_ge(s_ident, 1)
            nc.gpsimd.affine_select(out=ident[:, :], in_=ident[:, :], compare_op=ALU.not_equal, fill=1.0,
                                    base=0, pattern=[[-1, P]], channel_multiplier=1).then_inc(s_ident, 1)

            def add_rows(g, q, m, count, s):
                pool.wait_ge(s_lo, m * (2 * L) + 2 * q + 2)
                tile = raw[:, q % RAW, :].rearrange("p (k w) -> p k w", w=W)
                for k in range(SUB):
                    at = m * (SUB * BLOCKS) + SUB * count + k
                    if g == 0 and k == 0:
                        continue
                    if g == 0 and k == 1:
                        if count > 0:
                            pool.wait_ge(s_rows, at - 1)
                        nc.gpsimd.tensor_tensor(rows[:, :], tile[:, 0, :], tile[:, 1, :], ALU.add)\
                          .then_inc(s_rows, 2)
                        continue
                    pool.wait_ge(s_rows, at)
                    if g == BLOCKS - 1 and k == SUB - 1:
                        if not (isinstance(m, int) and s + m == 0):
                            pool.wait_ge(s_kout, m + s)
                        nc.gpsimd.tensor_tensor(rows_end[:, :], rows[:, :], tile[:, k, :], ALU.add)\
                          .then_inc(s_rows, 1)
                    else:
                        nc.gpsimd.tensor_tensor(rows[:, :], rows[:, :], tile[:, k, :], ALU.add)\
                          .then_inc(s_rows, 1)

            for g in range(HEAD):
                add_rows(g % BLOCKS, g, 0, g, g // BLOCKS)

            def one_pass(order, m):
                count = HEAD
                for q, (kind, g) in enumerate(order):
                    if kind == "T":
                        add_rows(g, HEAD + q, m, count, 1 if g >= LEAD else 2)
                        count += 1

            with pool.Fori(0, PASSES) as m:
                one_pass(BODY, m)
            one_pass(LAST_BODY, PASSES)

            pool.wait_ge(s_exp, 2)
            pool.wait_ge(s_kout, BLOCKS)
            for c in range(BLOCKS):
                if c:
                    pool.wait_ge(s_coef, c * (SUB + 1))
                for k in range(SUB):
                    nc.gpsimd.tensor_scalar(rows[:, k * P:(k + 1) * P], e1[:, :], e0[:, c * SUB + k:c * SUB + k + 1],
                                            None, ALU.mult).then_inc(s_coef, 1)
                pool.wait_ge(s_coef, c * (SUB + 1) + SUB)
                pool.wait_ge(s_added, (BLOCKS - 1) * BLOCKS + c + 1)
                nc.gpsimd.tensor_tensor(spec[:, c * W:(c + 1) * W], rows[:, :], spec[:, c * W:(c + 1) * W],
                                        ALU.mult).then_inc(s_coef, 1)

        @block.scalar
        def _(act):
            act.dma_start(k_sb[:, :], gnn_kernel).then_inc(s_const, 16)
            act.dma_start(bias_sb[:, :], bias.partition_broadcast(P)).then_inc(s_const, 16)
            act.dma_start(e0[:, :], evals0.partition_broadcast(P)).then_inc(s_const, 16)
            act.dma_start(e1[:, :], evals1.partition_broadcast(P)).then_inc(s_const, 16)
            act.dma_start(t_sb[:, :], times).then_inc(s_const, 16)
            act.wait_ge(s_negt, 1)
            nc.scalar.activation(e0[:, :], e0[:, :], ACT.Exp, scale=t_sb[:, 0:1]).then_inc(s_exp, 1)
            nc.scalar.activation(e1[:, :], e1[:, :], ACT.Exp, scale=t_sb[:, 1:2]).then_inc(s_exp, 1)

            def split(q, m):
                landed(act, q, m)
                for h in range(2):
                    if not (isinstance(m, int) and 2 * q + h + 2 * L * m < SPLIT):
                        act.wait_ge(s_half, m * (2 * L) + 2 * q + h - SPLIT + 1)
                    nc.scalar.activation(hi[:, (2 * q + h) % SPLIT, :], raw[:, q % RAW, h * HALF:(h + 1) * HALF],
                                         ACT.Copy).then_inc(s_hi, 1)

            def load_block(m, s):
                if not (isinstance(m, int) and s + m == 0):
                    act.wait_ge(s_y, m + s)
                act.dma_start(xi[:, :], x_blocks[bass.ds(m + s, 1), :, :].rearrange("a p n -> p (a n)"))\
                   .then_inc(s_xi, 16)
                act.dma_start(bm[:, :], beta_mass[bass.ds(m + s, 1), :, :].rearrange("a p n -> p (a n)"))\
                   .then_inc(s_xi, 16)

            def diag(m, s):
                act.wait_ge(s_xi, m * 32 + 32 * (s + 1))
                if not (isinstance(m, int) and s + m == 0):
                    act.wait_ge(s_x1, m * 16 + 16 * s)
                for k in range(SUB):
                    nc.scalar.activation(work[:, k * P:(k + 1) * P], ident[:, :], ACT.Copy,
                                         scale=bm[:, k:k + 1]).then_inc(s_diag, 1)

            def copy_agg(m, s, bank):
                act.wait_ge(s_agg, m + s + 1)
                nc.scalar.activation(work[:, :], acc[:, bank, :], ACT.Copy).then_inc(s_aggc, 1)

            def take_root(m, nth):
                act.wait_ge(s_var, m + nth + 1)
                nc.scalar.activation(root[:, :], var[:, :], ACT.Sqrt).then_inc(s_root, 1)

            def store_x1(m, s):
                act.wait_ge(s_y, m + s + 1)
                act.dma_start(x1_store[bass.ds(m + s, 1), :, :].rearrange("a p n -> p (a n)"), work[:, :])\
                   .then_inc(s_x1, 16)

            load_block(0, 0)
            for g in range(HEAD):
                if g < 4:
                    quarter = slice(g * N // 4, (g + 1) * N // 4)
                    act.wait_ge(s_x[g], 16)
                    nc.scalar.activation(w_hi[:, quarter], spec[:, quarter], ACT.Copy).then_inc(s_whi, 1)
                split(g, 0)
                if g == 4:
                    act.wait_ge(s_ident, 2)
                    diag(0, 0)
                if g == BLOCKS + 1:
                    copy_agg(0, 0, 1)
            take_root(0, 0)

            def one_pass(order, m, copy_at):
                for q, (kind, g) in enumerate(order):
                    split(HEAD + q, m)
                    if q == 4:
                        store_x1(m, 0)
                        load_block(m, 1)
                    if q == 10:
                        diag(m, 1)
                    if q == copy_at:
                        copy_agg(m, 1, 0)
                take_root(m, 1)

            A_END = BODY.index(("A", BLOCKS - 1))
            with act.Fori(0, PASSES) as m:
                one_pass(BODY, m, A_END)
            one_pass(LAST_BODY, PASSES, A_END - 1)

            def split_z(c):
                act.wait_ge(s_zt, c + 1)
                nc.scalar.activation(w_hi[:, c * W:(c + 1) * W], turned[:, c % 2, :], ACT.Copy).then_inc(s_zhi, 1)

            for e in range(2 * BLOCKS):
                split(TAIL + e, 0)
                if e == 1:
                    store_x1(0, BLOCKS - 1)
                if 0 <= e - Z_SPLIT < BLOCKS:
                    split_z(e - Z_SPLIT)

            def finish(g, m, j, b):
                if g == 0:
                    if j == 0:
                        act.wait_ge(s_zt, BLOCKS)
                        act.wait_ge(s_x1, 16 * BLOCKS)
                    act.dma_start(x1_in[:, b, :], x1_store[bass.ds(m * 2 + j, 1), :, :]
                                  .rearrange("a p n -> p (a n)")).then_inc(s_x1in[b], 16)
                if g == 1:
                    act.wait_ge(s_half, m * (2 * L) + 2 * (FINAL + (j + 1) * BLOCKS))
                    nc.scalar.activation(res_t[:, b, :], acc[:, b, :], ACT.Copy).then_inc(s_res, 1)
                if g == ROOT_AT:
                    take_root(m * 2, BLOCKS + j)
                if g == OUT_AT:
                    act.wait_ge(s_fin, m * 2 + j + 1)
                    act.dma_start(out_blocks[bass.ds(m * 2 + j, 1), :, :, :].rearrange("a p k f -> (a p) k f"),
                                  fin[:, b, :].rearrange("p (k f) -> p k f", f=F)).then_inc(s_out, 16)
                if g == BLOCKS - 1:
                    act.wait_ge(s_out, m * 32 + 16 * (j + 1))

            def final(q0, m, j, b):
                for g in range(BLOCKS):
                    split(q0 + g, m)
                    finish(g, m, j, b)

            with act.Fori(0, (BLOCKS - 2) // 2) as m:
                final(FINAL + BLOCKS, m, 0, 0)
                final(FINAL + 2 * BLOCKS, m, 1, 1)
            final(FINAL + (BLOCKS - 1) * BLOCKS, 0, BLOCKS - 2, 0)
            for g in range(BLOCKS):
                finish(g, 0, BLOCKS - 1, 1)

        @block.vector
        def _(dve):
            chain = [0]

            def link(ins, base):
                chain[0] += 1
                ins.then_inc(s_dve, 1)
                dve.wait_ge(s_dve, base + chain[0])

            def split(q, m):
                for h in range(2):
                    dve.wait_ge(s_hi, m * (2 * L) + 2 * q + h + 1)
                    nc.vector.tensor_tensor(lo[:, (2 * q + h) % SPLIT, :], raw[:, q % RAW, h * HALF:(h + 1) * HALF],
                                            hi[:, (2 * q + h) % SPLIT, :].bitcast(F32), ALU.subtract).then_inc(s_lo, 1)

            def add_part(m, c, q, m_chunks):
                dve.wait_ge(s_half, m_chunks * (2 * L) + 2 * q + 2)
                if c > 0:
                    dve.wait_ge(s_added, m * BLOCKS + c)
                here = spec[:, (c % BLOCKS) * W:(c % BLOCKS + 1) * W]
                nc.vector.tensor_tensor(here, part[:, c % 2, :], here, ALU.add).then_inc(s_added, 1)

            def statistics(src, base):
                for k in range(SUB):
                    ins = nc.vector.bn_stats(stats[:, k, :], src[:, k * F:(k + 1) * F])
                link(ins, base)
                nc.vector.tensor_tensor(mean[:, :], stats[:, :, 1], stats[:, :, 4], ALU.add)
                nc.vector.tensor_tensor(gap[:, :], stats[:, :, 1], stats[:, :, 4], ALU.subtract)
                link(nc.vector.tensor_tensor(var[:, :], stats[:, :, 2], stats[:, :, 5], ALU.add), base)
                nc.vector.tensor_scalar(mean[:, :], mean[:, :], 0.5, None, ALU.mult)
                nc.vector.tensor_scalar(var[:, :], var[:, :], 1.0 / F, EPS, ALU.mult, ALU.add)
                link(nc.vector.scalar_tensor_tensor(out=quot[:, :], in0=gap[:, :], scalar=0.25, in1=gap[:, :],
                                                    op0=ALU.mult, op1=ALU.mult), base)
                nc.vector.tensor_tensor(var[:, :], var[:, :], quot[:, :], ALU.add).then_inc(s_var, 1)

            def reciprocal_root(m, nth, base):
                dve.wait_ge(s_root, m + nth + 1)
                link(nc.vector.reciprocal(rstd[:, :], root[:, :]), base)
                link(nc.vector.tensor_tensor(quot[:, :], var[:, :], rstd[:, :], ALU.mult), base)
                link(nc.vector.tensor_tensor(quot[:, :], quot[:, :], root[:, :], ALU.add), base)
                link(nc.vector.tensor_scalar(quot[:, :], quot[:, :], 0.5, None, ALU.mult), base)
                link(nc.vector.reciprocal(rstd[:, :], quot[:, :]), base)

            def centre(dst, src, k):
                return nc.vector.tensor_scalar(dst[:, k * F:(k + 1) * F], src[:, k * F:(k + 1) * F],
                                               mean[:, k:k + 1], rstd[:, k:k + 1], ALU.subtract, ALU.mult)

            def layer0(m, s):
                chain[0] = 0
                base = m * CHAIN + s * CHAIN
                dve.wait_ge(s_kout, m + s + 1)
                dve.wait_ge(s_xi, m * 32 + 32 * (s + 1))
                link(nc.vector.tensor_tensor(deg[:, :], degp[:, 0:SUB], bm[:, 0:SUB], ALU.add), base)
                link(nc.vector.reciprocal(inv[:, :], deg[:, :]), base)
                for k in range(SUB):
                    cols = slice(k * F, (k + 1) * F)
                    ins = nc.vector.scalar_tensor_tensor(out=work[:, cols], in0=kout[:, cols], scalar=inv[:, k:k + 1],
                                                         in1=xi[:, cols], op0=ALU.mult, op1=ALU.add)
                link(ins, base)
                for k in range(SUB):
                    cols = slice(k * F, (k + 1) * F)
                    ins = nc.vector.tensor_tensor(work[:, cols], work[:, cols], bias_sb[:, :], ALU.add)
                link(ins, base)
                statistics(work, base)
                reciprocal_root(m, s, base)
                for k in range(SUB):
                    ins = centre(work, work, k)
                link(ins, base)
                for k in range(SUB):
                    cols = slice(k * F, (k + 1) * F)
                    ins = nc.vector.tensor_scalar(y_hi[:, cols], work[:, cols], bm[:, SUB + k:SUB + k + 1],
                                                  None, ALU.mult)
                link(ins, base)
                for k in range(SUB):
                    cols = slice(k * F, (k + 1) * F)
                    ins = nc.vector.scalar_tensor_tensor(out=y_lo[:, cols], in0=work[:, cols],
                                                         scalar=bm[:, SUB + k:SUB + k + 1],
                                                         in1=y_hi[:, cols].bitcast(F32),
                                                         op0=ALU.mult, op1=ALU.subtract)
                ins.then_inc(s_y, 1)
                assert chain[0] == CHAIN

            dve.wait_ge(s_const, 16 * CONSTS)
            nc.vector.tensor_scalar(t_sb[:, :], t_sb[:, :], -1.0, None, ALU.mult).then_inc(s_negt, 1)
            for g in range(HEAD):
                if g < 4:
                    quarter = slice(g * N // 4, (g + 1) * N // 4)
                    dve.wait_ge(s_whi, g + 1)
                    nc.vector.tensor_tensor(w_lo[:, quarter], spec[:, quarter], w_hi[:, quarter].bitcast(F32),
                                            ALU.subtract).then_inc(s_wlo, 1)
                split(g, 0)
                if g == 6:
                    dve.wait_ge(s_wlo, 4)
                    nc.vector.memset(spec[:, :], 0.0).then_inc(s_zero, 1)
            layer0(0, 0)
            dve.wait_ge(s_zero, 1)

            def one_pass(order, m):
                for q, (kind, g) in enumerate(order):
                    split(HEAD + q, m)
                    if q >= 2 and order[q - 2][0] == "A":
                        add_part(m, order[q - 2][1], HEAD + q - 2, m)
                for q in range(len(order) - 2, len(order)):
                    if order[q][0] == "A":
                        add_part(m, order[q][1], HEAD + q, m)
                layer0(m, 1)

            with dve.Fori(0, PASSES) as m:
                one_pass(BODY, m)
            one_pass(LAST_BODY, PASSES)

            for e in range(2 * BLOCKS):
                split(TAIL + e, 0)
                if 0 <= e - 2 < BLOCKS:
                    add_part(BLOCKS - 1, e - 2, TAIL + e - 2, 0)
                if 0 <= e - Z_SPLIT < BLOCKS:
                    c = e - Z_SPLIT
                    dve.wait_ge(s_zhi, c + 1)
                    nc.vector.tensor_tensor(w_lo[:, c * W:(c + 1) * W], turned[:, c % 2, :],
                                            w_hi[:, c * W:(c + 1) * W].bitcast(F32), ALU.subtract).then_inc(s_zlo, 1)

            def finish(g, m, j, b):
                base = BLOCKS * CHAIN + m * (2 * CHAIN_END) + j * CHAIN_END
                if g == SUM_AT:
                    chain[0] = 0
                    dve.wait_ge(s_rt, m * 2 + j + 1)
                    dve.wait_ge(s_x1in[b], m * 16 + 16 * (j // 2 + 1))
                    link(nc.vector.tensor_tensor(x1_in[:, b, :], turned[:, b, :], x1_in[:, b, :], ALU.add), base)
                    statistics(x1_in[:, b, :], base)
                if g == ROOT_AT:
                    reciprocal_root(m * 2, BLOCKS + j, base)
                    for k in range(SUB):
                        ins = centre(fin[:, b, :], x1_in[:, b, :], k)
                    ins.then_inc(s_fin, 1)
                    assert chain[0] == CHAIN_END

            def final(q0, m, j, b):
                for g in range(BLOCKS):
                    split(q0 + g, m)
                    finish(g, m, j, b)

            with dve.Fori(0, (BLOCKS - 2) // 2) as m:
                final(FINAL + BLOCKS, m, 0, 0)
                final(FINAL + 2 * BLOCKS, m, 1, 1)
            final(FINAL + (BLOCKS - 1) * BLOCKS, 0, BLOCKS - 2, 0)
            for g in range(BLOCKS):
                finish(g, 0, BLOCKS - 1, 1)

        @block.tensor
        def _(pe):
            def multiply(dst, left_hi, left_lo, first_tile, q, m, start, stop):
                for h in range(2):
                    at = (2 * q + h) % SPLIT
                    pe.wait_ge(s_hi, m * (2 * L) + 2 * q + h + 1)
                    for k in range(2):
                        cols = slice((first_tile + 2 * h + k) * P, (first_tile + 2 * h + k + 1) * P)
                        moving = hi[:, at, k * W:(k + 1) * W]
                        nc.tensor.matmul(dst, left_hi[:, cols], moving, start=(start and h == 0 and k == 0), stop=False)
                        nc.tensor.matmul(dst, left_lo[:, cols], moving, start=False, stop=False)
                    pe.wait_ge(s_lo, m * (2 * L) + 2 * q + h + 1)
                    for k in range(2):
                        cols = slice((first_tile + 2 * h + k) * P, (first_tile + 2 * h + k + 1) * P)
                        ins = nc.tensor.matmul(dst, left_hi[:, cols], lo[:, at, k * W:(k + 1) * W],
                                               start=False, stop=(stop and h == 1 and k == 1))
                    ins.then_inc(s_half, 1)

            def first_product(g, q, m, s, bank):
                if g == 0 and not (isinstance(m, int) and m + s < 2):
                    pe.wait_ge(s_aggc, m + s)
                multiply(acc[:, bank, :], w_hi, w_lo, SUB * g, q, m, g == 0, False)
                if g == BLOCKS - 1:
                    pe.wait_ge(s_diag, m * SUB + SUB * (s + 1))
                    for k in range(SUB):
                        cols = slice(k * P, (k + 1) * P)
                        ins = nc.tensor.matmul(acc[:, bank, cols], xi[:, cols], work[:, cols],
                                               start=False, stop=(k == SUB - 1))
                    ins.then_inc(s_agg, 1)

            def feature_product(m, s):
                pe.wait_ge(s_aggc, m + s + 1)
                pe.wait_ge(s_rows, m * (SUB * BLOCKS) + SUB * BLOCKS * (s + 1))
                for k in range(SUB):
                    cols = slice(k * P, (k + 1) * P)
                    nc.tensor.matmul(kout[:, k * F:(k + 1) * F], work[:, cols], k_sb[:, :], start=True, stop=True)
                for k in range(SUB):
                    ins = nc.tensor.matmul(degp[:, k:k + 1], rows_end[:, k * P:(k + 1) * P], ones[:, :],
                                           start=True, stop=True)
                ins.then_inc(s_kout, 1)

            def second_product(c, q, m, first):
                if first:
                    pe.wait_ge(s_y, m + 1)
                if c >= 2:
                    pe.wait_ge(s_added, m * BLOCKS + c - 1)
                multiply(part[:, c % 2, :], y_hi, y_lo, 0, q, m, True, True)

            pe.wait_ge(s_const, 16 * CONSTS)
            pe.wait_ge(s_ones, 1)
            for g in range(HEAD):
                if g < BLOCKS and g % 4 == 0:
                    pe.wait_ge(s_wlo, g // 4 + 1)
                first_product(g % BLOCKS, g, 0, g // BLOCKS, 1 - g // BLOCKS)
                if g == BLOCKS:
                    feature_product(0, 0)

            def one_pass(order, m):
                for q, (kind, g) in enumerate(order):
                    if kind == "A":
                        second_product(g, HEAD + q, m, g == 0)
                    elif g >= LEAD:
                        first_product(g, HEAD + q, m, 1, 0)
                    else:
                        first_product(g, HEAD + q, m, 2, 0)
                        if g == 0:
                            feature_product(m, 1)

            with pe.Fori(0, PASSES) as m:
                one_pass(BODY, m)
            one_pass(LAST_BODY, PASSES)
            feature_product(PASSES, 1)

            def third_product(g, q, m, bank):
                multiply(acc[:, bank, :], w_hi, w_lo, SUB * g, q, m, g == 0, g == BLOCKS - 1)

            for e in range(2 * BLOCKS):
                if e < BLOCKS:
                    if e == 0:
                        pe.wait_ge(s_y, BLOCKS)
                    if e >= 2:
                        pe.wait_ge(s_added, (BLOCKS - 1) * BLOCKS + e - 1)
                    multiply(part[:, e % 2, :], y_hi, y_lo, 0, TAIL + e, 0, True, True)
                else:
                    pe.wait_ge(s_zlo, e - BLOCKS + 1)
                    multiply(acc[:, 0, :], w_hi, w_lo, SUB * (e - BLOCKS), TAIL + e, 0,
                             e == BLOCKS, e == 2 * BLOCKS - 1)
                c = e - Z_TURN
                if 0 <= c < BLOCKS:
                    pe.wait_ge(s_coef, (c + 1) * (SUB + 1))
                    if c >= 2:
                        pe.wait_ge(s_zlo, c - 1)
                    for k in range(SUB):
                        at = c * W + k * P
                        turn = nc.tensor.transpose(turned[:, c % 2, k * P:(k + 1) * P], spec[:, at:at + P], ident[:, :])
                    turn.then_inc(s_zt, 1)
            def finish(g, m, j, b):
                if g == TURN_AT:
                    pe.wait_ge(s_res, m * 2 + j + 1)
                    for k in range(SUB):
                        cols = slice(k * P, (k + 1) * P)
                        turn = nc.tensor.transpose(turned[:, b, cols], res_t[:, b, cols], ident[:, :])
                    turn.then_inc(s_rt, 1)

            def final(q0, m, j, b):
                for g in range(BLOCKS):
                    multiply(acc[:, 1 - b, :], w_hi, w_lo, SUB * g, q0 + g, m, g == 0, g == BLOCKS - 1)
                    finish(g, m, j, b)

            with pe.Fori(0, (BLOCKS - 2) // 2) as m:
                final(FINAL + BLOCKS, m, 0, 0)
                final(FINAL + 2 * BLOCKS, m, 1, 1)
            final(FINAL + (BLOCKS - 1) * BLOCKS, 0, BLOCKS - 2, 0)
            finish(TURN_AT, 0, BLOCKS - 1, 1)


def kernel(**inputs):
    import numpy as np
    import concourse.bacc as bacc
    from concourse.bass_utils import run_bass_kernel_spmd

    adj = np.asarray(inputs["adj"])
    x = np.asarray(inputs["x"])
    beta_mass = np.stack([np.asarray(inputs["L0_gnn_beta"]), np.asarray(inputs["L1_gnn_mass"])])
    arrays = {
        "adj_t": adj.reshape(BLOCKS, W, BLOCKS, SUB, P).transpose(0, 2, 4, 3, 1).reshape(-1, P, CHUNK),
        "adj_n": adj.reshape(BLOCKS, SUB, P, BLOCKS, W).transpose(0, 3, 2, 1, 4).reshape(-1, P, CHUNK),
        "x_tiles": x.reshape(TILES, P, F).transpose(1, 0, 2).reshape(P, TILES * F),
        "x_blocks": x.reshape(BLOCKS, SUB, P, F).transpose(0, 2, 1, 3).reshape(BLOCKS, P, SUB * F),
        "beta_mass": beta_mass.reshape(2, BLOCKS, SUB, P).transpose(1, 3, 0, 2).reshape(BLOCKS, P, 2 * SUB),
        "gnn_kernel": np.asarray(inputs["L0_gnn_kernel"]),
        "bias": np.asarray(inputs["L0_gnn_bias"]),
        "evals0": np.asarray(inputs["L1_gnn_evals0"]),
        "evals1": np.asarray(inputs["L1_gnn_evals1"]),
        "times": np.asarray(inputs["L1_gnn_diffusion_time"]).T,
    }
    arrays = {name: np.ascontiguousarray(a) for name, a in arrays.items()}
    nc = bacc.Bacc("TRN2", target_bir_lowering=False, num_devices=1)
    args = [nc.dram_tensor(name, a.shape, F32, kind="ExternalInput").ap() for name, a in arrays.items()]
    args.append(nc.dram_tensor("x1_store", (BLOCKS, P, SUB * F), F32).ap())
    args.append(nc.dram_tensor("out", (N, F), F32, kind="ExternalOutput").ap())
    build(nc, *args)
    result = run_bass_kernel_spmd(nc, [arrays], core_ids=[0])
    return result.results[0]["out"]
```

```python
from contextlib import ExitStack

import concourse.bass as bass
from concourse import mybir

F32 = mybir.dt.float32
F32R = mybir.dt.float32r
ALU = mybir.AluOpType
ACT = mybir.ActivationFunctionType
AX = mybir.AxisListType

P = 128
N = 8192
F = 128
W = 512
TILES = N // P
BLOCKS = N // W
SUB = W // P
CHUNK = SUB * W
HALF = CHUNK // 2
RAW = 8
SPLIT = 4
LEAD = 3
HELD = 2
EPS = 1e-5

BODY = [("A", c) for c in range(HELD)]
for i in range(BLOCKS - LEAD - HELD):
    BODY += [("A", HELD + i), ("T", LEAD + i)]
BODY += [("T", t) for t in range(BLOCKS - HELD, BLOCKS)]
BODY += [("A", BLOCKS - 3), ("T", 0), ("A", BLOCKS - 2), ("A", BLOCKS - 1)] + [("T", t) for t in range(1, LEAD)]
LEFT_OUT = 3, 6, 9
LAST_BODY = [("A", c) for c in range(HELD)]
for i in range(BLOCKS - LEAD - HELD):
    a = ("A", HELD + i - sum(at < i for at in LEFT_OUT))
    LAST_BODY += [None if i in LEFT_OUT else a, ("T", LEAD + i)]
LAST_BODY += [("T", t) for t in range(BLOCKS - HELD, BLOCKS)]
LAST_BODY += [("A", c) for c in range(BLOCKS - (RAW - HELD), BLOCKS)]
assert BODY.index(("T", BLOCKS - HELD)) == LAST_BODY.index(("T", BLOCKS - HELD)) and len(LAST_BODY) == len(BODY)
L = len(BODY)
assert L == 2 * BLOCKS and BODY.index(("T", BLOCKS - HELD)) + RAW == L and L % RAW == 0
GAP_HEAD = RAW - HELD - LEAD
HEAD = BLOCKS + GAP_HEAD + LEAD
PASSES = BLOCKS - 2
LAST = HEAD + PASSES * L
TAIL = LAST + L
FINAL = TAIL + BLOCKS

ITEMS = [("T", t) for t in range(BLOCKS)] + [None] * GAP_HEAD + [("T", t) for t in range(LEAD)]
ITEMS += BODY * PASSES + LAST_BODY
ITEMS += [("A", c) for c in range(BLOCKS)] + [("Z", g) for g in range(BLOCKS * BLOCKS)]


def is_loaded(n):
    return ITEMS[n] is not None and not (ITEMS[n][0] == "A" and ITEMS[n][1] < HELD)


def is_turned(item):
    return item[0] == "T" and item[1] >= BLOCKS - HELD


LOADS = [sum(is_loaded(n) for n in range(at % RAW, at + 1, RAW)) for at in range(len(ITEMS))]


def running(marks):
    counts, count = [], 0
    for mark in marks:
        count += bool(mark)
        counts.append(count)
    return counts


STEPS = running(item is not None and item[0] == "T" and not is_turned(item) for item in ITEMS)
GPSIMD_LOW = {("A", c) for c in (1, 14, 15)}
BY_GPSIMD = [h == 1 and n < LAST and ITEMS[n] in GPSIMD_LOW for n in range(len(ITEMS)) for h in range(2)]
LOW_GPSIMD = running(BY_GPSIMD)
LOW_VECTOR = running(ITEMS[u // 2] is not None and not BY_GPSIMD[u] for u in range(len(BY_GPSIMD)))


def missing_after(n):
    count = 0
    while n + 1 + count < len(ITEMS) and ITEMS[n + 1 + count] is None:
        count += 1
    return count


def build(nc, adj_t, adj_n, x_tiles, x_blocks, beta_mass, gnn_kernel, bias, evals0, evals1, times, x1_store, out):
    with ExitStack() as ctx:
        def sb(name, shape, dt=F32):
            return ctx.enter_context(nc.sbuf_tensor(name, shape, dt))

        def pb(name, shape):
            return ctx.enter_context(nc.psum_tensor(name, shape, F32))

        def sem(name):
            return ctx.enter_context(nc.semaphore(name))

        raw = sb("raw", [P, RAW, CHUNK])
        hi = sb("hi", [P, SPLIT, HALF], F32R)
        lo = sb("lo", [P, SPLIT, HALF], F32R)
        w_hi = sb("w_hi", [P, TILES * F], F32R)
        w_lo = sb("w_lo", [P, TILES * F], F32R)
        spec = sb("spec", [P, N])
        y_hi = sb("y_hi", [P, W], F32R)
        y_lo = sb("y_lo", [P, W], F32R)
        xi = sb("xi", [P, W])
        work = sb("work", [P, W])
        rows = sb("rows", [P, 2 * W])
        held_sums = sb("held_sums", [P, SUB, HELD])
        unused = sb("unused", [P, W], mybir.dt.bfloat16)
        k_sb = sb("k_sb", [P, F])
        bias_sb = sb("bias_sb", [P, F])
        ident = sb("ident", [P, P])
        ones = sb("ones", [P, 1])
        t_sb = sb("t_sb", [P, 2])
        bm = sb("bm", [P, 2 * SUB])
        e0 = xi[:, 0:TILES]
        e1 = xi[:, TILES:TILES + P]
        deg = sb("deg", [P, SUB])
        deg_held = sb("deg_held", [P, SUB])
        inv = sb("inv", [P, SUB])
        stats = sb("stats", [P, SUB, 6])
        mean = sb("mean", [P, SUB])
        gap = sb("gap", [P, SUB])
        var = sb("var", [P, SUB])
        root = sb("root", [P, SUB])
        quot = sb("quot", [P, SUB])
        rstd = sb("rstd", [P, SUB])
        shift = sb("shift", [P, SUB])
        res_t = spec[:, 0:2 * W].rearrange("p (b w) -> p b w", b=2)
        x1_in = spec[:, 2 * W:4 * W].rearrange("p (b w) -> p b w", b=2)
        fin = spec[:, 4 * W:6 * W].rearrange("p (b w) -> p b w", b=2)

        acc = pb("acc", [P, W])
        part = pb("part", [P, 2, W])
        turned = pb("turned", [P, 4, W])
        kout = pb("kout", [P, W])
        degp = turned[:, 3, 0:SUB]
        acc_end = [acc, kout]

        s_raw = [sem(f"s_raw{i}") for i in range(RAW)]
        s_hi = sem("s_hi")
        s_lo = sem("s_lo")
        s_lo_pool = sem("s_lo_pool")
        s_half = sem("s_half")
        s_rows = sem("s_rows")
        s_x = [sem(f"s_quarter{i}") for i in range(4)]
        s_whi = sem("s_whi")
        s_wlo = sem("s_wlo")
        s_zero = sem("s_zero")
        s_deg = sem("s_deg")
        s_share = sem("s_share")
        s_held = sem("s_held")
        s_xb = sem("s_xb")
        s_turn = sem("s_turn")
        s_evals = sem("s_evals")
        s_const = sem("s_const")
        s_ones = sem("s_ones")
        s_ident = sem("s_ident")
        s_negt = sem("s_negt")
        s_exp = sem("s_exp")
        s_xi = sem("s_xi")
        s_diag = sem("s_diag")
        s_agg = sem("s_agg")
        s_aggc = sem("s_aggc")
        s_kout = sem("s_kout")
        s_dve = sem("s_dve")
        s_var = sem("s_var")
        s_root = sem("s_root")
        s_y = sem("s_y")
        s_x1 = sem("s_x1")
        s_added = sem("s_added")
        s_norm = sem("s_norm")
        s_xn = sem("s_xn")
        s_yhi = sem("s_yhi")
        s_coef = sem("s_coef")
        s_zt = sem("s_zt")
        s_zhi = sem("s_zhi")
        s_zlo = sem("s_zlo")
        s_res = sem("s_res")
        s_rt = sem("s_rt")
        s_x1in = [sem("s_x1in0"), sem("s_x1in1")]
        s_fin = sem("s_fin")
        s_out = sem("s_out")

        CONSTS = 3
        CHAIN = 11
        CHAIN_END = 8
        FEATURES_AT = BODY.index(("T", 0)) - 1
        CHAIN_AT = L - 4, L - 3, L - 2
        TURN_AT, SUM_AT, ROOT_AT, OUT_AT = 3, 6, 8, 11
        Z_TURN, Z_SPLIT = 11, 14
        out_blocks = out.rearrange("(b k p) f -> b p k f", k=SUB, p=P)

        block = ctx.enter_context(nc.Block())


        def landed(eng, q, m):
            per_pass = 0 if isinstance(m, int) else LOADS[q + L] - LOADS[q]
            eng.wait_ge(s_raw[q % RAW], m * (16 * per_pass) + 16 * LOADS[q])

        def halves(q, m, h):
            return m * (2 * L) + 2 * q + h + 1

        def turns(q, m, h):
            count = sum(item is not None and is_turned(item) for item in ITEMS[:q])
            return m * (2 * HELD) + 2 * count + h + 1

        def wait_low(eng, q, m, h):
            u = 2 * q + h
            done, counts = (s_lo_pool, LOW_GPSIMD) if BY_GPSIMD[u] else (s_lo, LOW_VECTOR)
            per_pass = 0 if isinstance(m, int) else counts[u + 2 * L] - counts[u]
            eng.wait_ge(done, m * per_pass + counts[u])

        def step_for(q, h):
            return 1 + (2 * missing_after(q) if h else 0)

        @block.sync
        def _(sp):
            def load(src, index, q, m):
                in_loop = not isinstance(m, int)
                before = (q + L if in_loop else q) - RAW
                while before >= 0 and ITEMS[before] is None:
                    before -= RAW
                if before >= 0:
                    u = 2 * before + 1
                    if ITEMS[before][0] == "T":
                        done, count, per_pass = s_rows, 2 * STEPS[before], 2 * (BLOCKS - HELD)
                    elif BY_GPSIMD[u]:
                        done, count, per_pass = s_lo_pool, LOW_GPSIMD[u], len(GPSIMD_LOW)
                    elif before < LAST:
                        done, count, per_pass = s_lo, LOW_VECTOR[u], 2 * L - len(GPSIMD_LOW)
                    else:
                        done, count, per_pass = s_lo, LOW_VECTOR[u], 2 * L
                    sp.wait_ge(done, m * per_pass + count - per_pass if in_loop else count)
                sp.dma_start(raw[:, q % RAW, :], src[bass.ds(index, 1), :, :].rearrange("a p n -> p (a n)"))\
                  .then_inc(s_raw[q % RAW], 16)

            def load_step(t, block_at, q, m):
                if t < BLOCKS - HELD:
                    load(adj_t, block_at + t + HELD, q, m)
                else:
                    load(adj_n, block_at + t + HELD - BLOCKS, q, m)

            for n in range(HEAD):
                if n < 4:
                    quarter = slice(n * N // 4, (n + 1) * N // 4)
                    sp.dma_start(spec[:, quarter], x_tiles[:, quarter]).then_inc(s_x[n], 16)
                if ITEMS[n] is not None:
                    load_step(ITEMS[n][1], BLOCKS * (n >= BLOCKS), n, 0)

            def one_pass(order, q0, m, block_at):
                for q, item in enumerate(order):
                    if item is None:
                        continue
                    kind, t = item
                    if kind == "A":
                        if t >= HELD:
                            load(adj_n, block_at + t, q0 + q, m)
                    else:
                        load_step(t, block_at + (BLOCKS if t >= LEAD else 2 * BLOCKS), q0 + q, m)

            one_pass(BODY, HEAD, 0, 0)
            with sp.Fori(1, PASSES) as m:
                one_pass(BODY, HEAD, m, m * BLOCKS)
            one_pass(LAST_BODY, LAST, 0, PASSES * BLOCKS)
            for c in range(HELD, BLOCKS):
                load(adj_n, (BLOCKS - 1) * BLOCKS + c, TAIL + c, 0)

            def final(q0, m, first):
                for g in range(BLOCKS):
                    load(adj_t, m * (2 * BLOCKS) + first + g, q0 + g, m)

            final(FINAL, 0, 0)
            with sp.Fori(0, (BLOCKS - 2) // 2) as m:
                final(FINAL + BLOCKS, m, BLOCKS)
                final(FINAL + 2 * BLOCKS, m, 2 * BLOCKS)
            final(FINAL + (BLOCKS - 1) * BLOCKS, 0, (BLOCKS - 1) * BLOCKS)
            sp.wait_ge(s_out, 16 * BLOCKS)
            sp.wait_ge(s_x1, 16 * BLOCKS)

        @block.gpsimd
        def _(pool):
            nc.gpsimd.memset(ones[:, :], 1.0).then_inc(s_ones, 1)
            nc.gpsimd.memset(ident[:, :], 0.0).then_inc(s_ident, 1)
            pool.wait_ge(s_ident, 1)
            nc.gpsimd.affine_select(out=ident[:, :], in_=ident[:, :], compare_op=ALU.not_equal, fill=1.0,
                                    base=0, pattern=[[-1, P]], channel_multiplier=1).then_inc(s_ident, 1)

            def add_rows(t, q, m, s, only=None):
                landed(pool, q, m)
                before = m * (2 * (BLOCKS - HELD)) + 2 * (STEPS[q] - 1)
                head = isinstance(m, int) and m + s == 0
                first, second = raw[:, q % RAW, 0:HALF], raw[:, q % RAW, HALF:CHUNK]
                if t == 0:
                    if not head:
                        pool.wait_ge(s_deg, m + s)
                    wait_low(pool, q, m, 1)
                    nc.gpsimd.tensor_tensor(rows[:, :], first, second, ALU.add).then_inc(s_rows, 2)
                    return
                if only != 1:
                    pool.wait_ge(s_rows, before)
                    nc.gpsimd.tensor_tensor(rows[:, :], rows[:, :], first, ALU.add).then_inc(s_rows, 1)
                if only == 0:
                    return
                pool.wait_ge(s_rows, before + 1)
                wait_low(pool, q, m, 1)
                if head:
                    pool.wait_ge(s_share, t)
                    nc.gpsimd.tensor_tensor(rows[:, 0:W], rows[:, 0:W], second[:, 0:W], ALU.add).then_inc(s_rows, 1)
                else:
                    nc.gpsimd.tensor_tensor(rows[:, :], rows[:, :], second, ALU.add).then_inc(s_rows, 1)

            def low(q, m):
                pool.wait_ge(s_hi, halves(q, m, 1))
                wait_low(pool, q, m, 0)
                u = 2 * q + 1
                nc.gpsimd.tensor_tensor(lo[:, u % SPLIT, :], raw[:, q % RAW, HALF:CHUNK],
                                        hi[:, u % SPLIT, :].bitcast(F32), ALU.subtract).then_inc(s_lo_pool, 1)

            def add_bias(m, s):
                pool.wait_ge(s_agg, m + s + 1)
                nc.gpsimd.tensor_tensor(xi[:, :].rearrange("p (k f) -> p k f", f=F),
                                        xi[:, :].rearrange("p (k f) -> p k f", f=F),
                                        bias_sb[:, :].unsqueeze(1).to_broadcast([P, SUB, F]), ALU.add).then_inc(s_xb, 1)

            pool.wait_ge(s_const, 16 * CONSTS)
            for n in range(HEAD):
                if ITEMS[n] is not None and not is_turned(ITEMS[n]):
                    add_rows(ITEMS[n][1], n, 0, n // BLOCKS)
                if n == BLOCKS:
                    add_bias(0, 0)

            def one_pass(order, q0, m, s):
                for q, item in enumerate(order):
                    if item is not None and item[0] == "T" and not is_turned(item):
                        t = item[1]
                        add_rows(t, q0 + q, m, s + (0 if t >= LEAD else 1), 1 if t == 1 else None)
                    if item == ("A", BLOCKS - 1) and order is BODY:
                        add_rows(1, q0 + q + 1, m, s + 1, 0)
                    if BY_GPSIMD[2 * (q0 + q) + 1]:
                        low(q0 + q, m)
                    if q == FEATURES_AT:
                        add_bias(m, s)

            with pool.Fori(0, PASSES) as m:
                one_pass(BODY, HEAD, m, 1)
            one_pass(LAST_BODY, LAST, 0, BLOCKS - 1)

            pool.wait_ge(s_exp, 2)
            pool.wait_ge(s_y, BLOCKS)
            for c in range(BLOCKS):
                if c:
                    pool.wait_ge(s_coef, 2 * c)
                nc.gpsimd.tensor_tensor(rows[:, 0:W].rearrange("p (k f) -> p k f", f=P),
                                        e1.unsqueeze(1).to_broadcast([P, SUB, P]),
                                        e0[:, c * SUB:(c + 1) * SUB].unsqueeze(2).to_broadcast([P, SUB, P]),
                                        ALU.mult).then_inc(s_coef, 1)
                pool.wait_ge(s_coef, 2 * c + 1)
                pool.wait_ge(s_added, (BLOCKS - 1) * BLOCKS + c + 2)
                nc.gpsimd.tensor_tensor(spec[:, c * W:(c + 1) * W], rows[:, 0:W], spec[:, c * W:(c + 1) * W],
                                        ALU.mult).then_inc(s_coef, 1)

        @block.scalar
        def _(act):
            act.dma_start(k_sb[:, :], gnn_kernel).then_inc(s_const, 16)
            act.dma_start(bias_sb[:, :], bias.partition_broadcast(P)).then_inc(s_const, 16)
            act.dma_start(t_sb[:, :], times).then_inc(s_const, 16)

            def split(q, m, item, between=None):
                turn = is_turned(item)
                if not turn:
                    landed(act, q, m)
                for h in range(2):
                    if not (isinstance(m, int) and 2 * q + h < SPLIT):
                        act.wait_ge(s_half, halves(q, m, h) - SPLIT)
                    if turn:
                        act.wait_ge(s_turn, turns(q, m, h))
                        src = turned[:, 2 * h:2 * h + 2, :].rearrange("p a w -> p (a w)")
                    else:
                        src = raw[:, q % RAW, h * HALF:(h + 1) * HALF]
                    nc.scalar.activation(hi[:, (2 * q + h) % SPLIT, :], src, ACT.Copy).then_inc(s_hi, step_for(q, h))
                    if h == 0 and between is not None:
                        between()
                    if sums:
                        held_row_sum(m, *sums.pop(0))
                if turn:
                    sums.extend((q, item[1] - BLOCKS + HELD, k) for k in range(SUB))
                    held_row_sum(m, *sums.pop(0))

            sums = []

            def held_row_sum(m, q, i, k):
                before = SUB * sum(item is not None and is_turned(item) for item in ITEMS[:q]) + k
                if before > 0:
                    act.wait_ge(s_held, m * (SUB * HELD) + before)
                nc.scalar.activation(unused[:, :], raw[:, q % RAW, k * W:(k + 1) * W], ACT.Copy,
                                     accum_out=held_sums[:, k, i:i + 1]).then_inc(s_held, 1)

            def load_block(m, s):
                if not (isinstance(m, int) and s + m == 0):
                    act.wait_ge(s_y, m + s)
                act.dma_start(xi[:, :], x_blocks[bass.ds(m + s, 1), :, :].rearrange("a p n -> p (a n)"))\
                   .then_inc(s_xi, 16)
                act.dma_start(bm[:, :], beta_mass[bass.ds(m + s, 1), :, :].rearrange("a p n -> p (a n)"))\
                   .then_inc(s_xi, 16)

            def diag(m, s):
                act.wait_ge(s_xi, m * 32 + 32 * (s + 1))
                if not (isinstance(m, int) and s + m == 0):
                    act.wait_ge(s_x1, m * 16 + 16 * s)
                for k in range(SUB):
                    nc.scalar.activation(work[:, k * P:(k + 1) * P], ident[:, :], ACT.Copy,
                                         scale=bm[:, k:k + 1]).then_inc(s_diag, 1)

            def copy_agg(m, s, bank):
                act.wait_ge(s_agg, m + s + 1)
                nc.scalar.activation(work[:, :], bank, ACT.Copy).then_inc(s_aggc, 1)

            def take_root(m, nth):
                act.wait_ge(s_var, m + nth + 1)
                nc.scalar.activation(root[:, :], var[:, :], ACT.Sqrt).then_inc(s_root, 1)

            def normalise(m, s):
                act.wait_ge(s_norm, m + s + 1)
                for k in range(SUB):
                    cols = slice(k * F, (k + 1) * F)
                    nc.scalar.activation(work[:, cols], work[:, cols], ACT.Identity, scale=rstd[:, k:k + 1],
                                         bias=shift[:, k:k + 1]).then_inc(s_xn, 1)

            def mass_high(m, s, last_a):
                act.wait_ge(s_xn, m * SUB + SUB * (s + 1))
                if last_a is not None:
                    act.wait_ge(s_half, last_a)
                for k in range(SUB):
                    cols = slice(k * F, (k + 1) * F)
                    nc.scalar.activation(y_hi[:, cols], work[:, cols], ACT.Copy, scale=bm[:, SUB + k:SUB + k + 1])\
                      .then_inc(s_yhi, 1)

            def store_x1(m, s):
                act.wait_ge(s_y, m + s + 1)
                act.dma_start(x1_store[bass.ds(m + s, 1), :, :].rearrange("a p n -> p (a n)"), work[:, :])\
                   .then_inc(s_x1, 16)

            load_block(0, 0)
            for n in range(HEAD):
                if n < 4:
                    quarter = slice(n * N // 4, (n + 1) * N // 4)
                    act.wait_ge(s_x[n], 16)
                    nc.scalar.activation(w_hi[:, quarter], spec[:, quarter], ACT.Copy).then_inc(s_whi, 1)
                if ITEMS[n] is not None:
                    split(n, 0, ITEMS[n])
                if 7 <= n < 7 + N // HALF:
                    if n == 7:
                        act.wait_ge(s_wlo, 4)
                    here = spec[:, (n - 7) * HALF:(n - 6) * HALF]
                    nc.scalar.activation(here, here, ACT.Copy, scale=0.0)\
                      .then_inc(s_zero if n < 6 + N // HALF else s_added, 1)
                if n == 4:
                    act.wait_ge(s_ident, 2)
                    diag(0, 0)
                if n == HEAD - 2:
                    copy_agg(0, 0, part[:, 0, :])
            while sums:
                held_row_sum(0, *sums.pop(0))
            take_root(0, 0)
            normalise(0, 0)
            mass_high(0, 0, None)

            def one_pass(order, q0, m, s):
                for q, item in enumerate(order):
                    between = None
                    if q == L - 1 and item == BODY[-1]:
                        between = lambda: mass_high(m, s + 1, halves(q0 + BODY.index(("A", BLOCKS - 1)), m, 1))
                    if item is not None:
                        split(q0 + q, m, item, between)
                    if q == 4:
                        store_x1(m, s)
                        load_block(m, s + 1)
                    if q == 10:
                        diag(m, s + 1)
                    if q == FEATURES_AT + 1:
                        copy_agg(m, s + 1, acc[:, :])
                    if q == L - 3:
                        take_root(m, s + 1)
                    if q == L - 2:
                        normalise(m, s + 1)
                if order is LAST_BODY:
                    mass_high(m, s + 1, halves(q0 + L - 1, m, 1))
                assert not sums

            with act.Fori(0, PASSES) as m:
                one_pass(BODY, HEAD, m, 0)
            one_pass(LAST_BODY, LAST, 0, PASSES)

            def split_z(c):
                act.wait_ge(s_zt, c + 1)
                nc.scalar.activation(w_hi[:, c * W:(c + 1) * W], turned[:, c % 4, :], ACT.Copy).then_inc(s_zhi, 1)

            for e in range(2 * BLOCKS):
                split(TAIL + e, 0, ITEMS[TAIL + e])
                if e == 0:
                    store_x1(0, BLOCKS - 1)
                    act.dma_start(e0, evals0.partition_broadcast(P)).then_inc(s_evals, 16)
                    act.dma_start(e1, evals1.partition_broadcast(P)).then_inc(s_evals, 16)
                if e == 1:
                    act.wait_ge(s_negt, 1)
                    act.wait_ge(s_evals, 32)
                    nc.scalar.activation(e0, e0, ACT.Exp, scale=t_sb[:, 0:1]).then_inc(s_exp, 1)
                    nc.scalar.activation(e1, e1, ACT.Exp, scale=t_sb[:, 1:2]).then_inc(s_exp, 1)
                if 0 <= e - Z_SPLIT < BLOCKS:
                    split_z(e - Z_SPLIT)

            def finish(g, m, j, b):
                if g == 0:
                    if j == 0:
                        act.wait_ge(s_zt, BLOCKS)
                        act.wait_ge(s_x1, 16 * BLOCKS)
                    act.dma_start(x1_in[:, b, :], x1_store[bass.ds(m * 2 + j, 1), :, :]
                                  .rearrange("a p n -> p (a n)")).then_inc(s_x1in[b], 16)
                if g == 1:
                    act.wait_ge(s_half, halves(FINAL + (j + 1) * BLOCKS - 1, m, 1))
                    nc.scalar.activation(res_t[:, b, :], acc_end[b][:, :], ACT.Copy).then_inc(s_res, 1)
                if g == ROOT_AT:
                    take_root(m * 2, BLOCKS + j)
                if g == OUT_AT:
                    act.wait_ge(s_fin, m * 2 + j + 1)
                    act.dma_start(out_blocks[bass.ds(m * 2 + j, 1), :, :, :].rearrange("a p k f -> (a p) k f"),
                                  fin[:, b, :].rearrange("p (k f) -> p k f", f=F)).then_inc(s_out, 16)
                if g == BLOCKS - 1:
                    act.wait_ge(s_out, m * 32 + 16 * (j + 1))

            def final(q0, m, j, b):
                for g in range(BLOCKS):
                    split(q0 + g, m, ("Z", g))
                    finish(g, m, j, b)

            with act.Fori(0, (BLOCKS - 2) // 2) as m:
                final(FINAL + BLOCKS, m, 0, 0)
                final(FINAL + 2 * BLOCKS, m, 1, 1)
            final(FINAL + (BLOCKS - 1) * BLOCKS, 0, BLOCKS - 2, 0)
            for g in range(BLOCKS):
                finish(g, 0, BLOCKS - 1, 1)

        @block.vector
        def _(dve):
            chain = [0]

            def link(ins, base):
                chain[0] += 1
                ins.then_inc(s_dve, 1)
                dve.wait_ge(s_dve, base + chain[0])

            def split(q, m, item, between=None):
                for h in range(2):
                    if h == 1 and between is not None:
                        between()
                    if BY_GPSIMD[2 * q + h]:
                        continue
                    dve.wait_ge(s_hi, halves(q, m, h))
                    if is_turned(item):
                        src = turned[:, 2 * h:2 * h + 2, :].rearrange("p a w -> p (a w)")
                    else:
                        src = raw[:, q % RAW, h * HALF:(h + 1) * HALF]
                    nc.vector.tensor_tensor(lo[:, (2 * q + h) % SPLIT, :], src,
                                            hi[:, (2 * q + h) % SPLIT, :].bitcast(F32), ALU.subtract)\
                      .then_inc(s_lo, 1)

            def add_part(m, s, c, q):
                dve.wait_ge(s_half, halves(q, m, 1))
                dve.wait_ge(s_added, m * BLOCKS + s * BLOCKS + c + 1)
                here = spec[:, (c % BLOCKS) * W:(c % BLOCKS + 1) * W]
                nc.vector.tensor_tensor(here, part[:, c % 2, :], here, ALU.add).then_inc(s_added, 1)

            def statistics(src, base):
                for k in range(SUB):
                    ins = nc.vector.bn_stats(stats[:, k, :], src[:, k * F:(k + 1) * F])
                link(ins, base)
                nc.vector.tensor_tensor(mean[:, :], stats[:, :, 1], stats[:, :, 4], ALU.add)
                nc.vector.tensor_tensor(gap[:, :], stats[:, :, 1], stats[:, :, 4], ALU.subtract)
                link(nc.vector.tensor_tensor(var[:, :], stats[:, :, 2], stats[:, :, 5], ALU.add), base)
                nc.vector.tensor_scalar(mean[:, :], mean[:, :], 0.5, None, ALU.mult)
                nc.vector.tensor_scalar(var[:, :], var[:, :], 1.0 / F, EPS, ALU.mult, ALU.add)
                link(nc.vector.scalar_tensor_tensor(out=quot[:, :], in0=gap[:, :], scalar=0.25, in1=gap[:, :],
                                                    op0=ALU.mult, op1=ALU.mult), base)
                nc.vector.tensor_tensor(var[:, :], var[:, :], quot[:, :], ALU.add).then_inc(s_var, 1)

            def reciprocal_root(m, nth, base):
                dve.wait_ge(s_root, m + nth + 1)
                link(nc.vector.reciprocal(rstd[:, :], root[:, :]), base)
                link(nc.vector.scalar_tensor_tensor(out=quot[:, :], in0=var[:, :], scalar=0.5, in1=rstd[:, :],
                                                    op0=ALU.mult, op1=ALU.mult), base)
                link(nc.vector.scalar_tensor_tensor(out=quot[:, :], in0=root[:, :], scalar=0.5, in1=quot[:, :],
                                                    op0=ALU.mult, op1=ALU.add), base)
                link(nc.vector.reciprocal(rstd[:, :], quot[:, :]), base)

            def centre(dst, src, k):
                return nc.vector.tensor_scalar(dst[:, k * F:(k + 1) * F], src[:, k * F:(k + 1) * F],
                                               mean[:, k:k + 1], rstd[:, k:k + 1], ALU.subtract, ALU.mult)

            def layer0_degree(m, s):
                chain[0] = 0
                base = m * CHAIN + s * CHAIN
                dve.wait_ge(s_deg, m + s + 1)
                dve.wait_ge(s_xi, m * 32 + 32 * (s + 1))
                dve.wait_ge(s_held, m * (SUB * HELD) + SUB * HELD * (s + 1))
                nc.vector.tensor_reduce(deg_held[:, :], held_sums[:, :, :], AX.X, ALU.add)
                link(nc.vector.tensor_tensor(deg[:, :], degp, bm[:, 0:SUB], ALU.add), base)
                link(nc.vector.tensor_tensor(deg[:, :], deg[:, :], deg_held[:, :], ALU.add), base)
                link(nc.vector.reciprocal(inv[:, :], deg[:, :]), base)

            def layer0_sum(m, s):
                base = m * CHAIN + s * CHAIN
                dve.wait_ge(s_kout, m + s + 1)
                dve.wait_ge(s_xb, m + s + 1)
                for k in range(SUB):
                    cols = slice(k * F, (k + 1) * F)
                    ins = nc.vector.scalar_tensor_tensor(out=work[:, cols], in0=kout[:, cols], scalar=inv[:, k:k + 1],
                                                         in1=xi[:, cols], op0=ALU.mult, op1=ALU.add)
                link(ins, base)
                statistics(work, base)

            def layer0_scales(m, s):
                base = m * CHAIN + s * CHAIN
                reciprocal_root(m, s, base)
                nc.vector.scalar_tensor_tensor(out=shift[:, :], in0=mean[:, :], scalar=-1.0, in1=rstd[:, :],
                                               op0=ALU.mult, op1=ALU.mult).then_inc(s_norm, 1)

            def layer0_mass_low(m, s):
                dve.wait_ge(s_yhi, m * SUB + SUB * (s + 1))
                for k in range(SUB):
                    cols = slice(k * F, (k + 1) * F)
                    ins = nc.vector.scalar_tensor_tensor(out=y_lo[:, cols], in0=work[:, cols],
                                                         scalar=bm[:, SUB + k:SUB + k + 1],
                                                         in1=y_hi[:, cols].bitcast(F32),
                                                         op0=ALU.mult, op1=ALU.subtract)
                ins.then_inc(s_y, 1)
                assert chain[0] == CHAIN

            LAYER0 = [layer0_degree, layer0_sum, layer0_scales, layer0_mass_low]

            dve.wait_ge(s_const, 16 * CONSTS)
            nc.vector.tensor_scalar(t_sb[:, :], t_sb[:, :], -1.0, None, ALU.mult).then_inc(s_negt, 1)
            for n in range(HEAD):
                if n < 4:
                    quarter = slice(n * N // 4, (n + 1) * N // 4)
                    dve.wait_ge(s_whi, n + 1)
                    nc.vector.tensor_tensor(w_lo[:, quarter], spec[:, quarter], w_hi[:, quarter].bitcast(F32),
                                            ALU.subtract).then_inc(s_wlo, 1)
                if ITEMS[n] is not None:
                    split(n, 0, ITEMS[n])
                if 1 <= n < BLOCKS - HELD:
                    tile = raw[:, n % RAW, (SUB - 1) * W:SUB * W]
                    if n == 1:
                        nc.vector.tensor_copy(kout[:, :], tile).then_inc(s_share, 1)
                    else:
                        dve.wait_ge(s_share, n - 1)
                        nc.vector.tensor_tensor(kout[:, :], kout[:, :], tile, ALU.add).then_inc(s_share, 1)
                if n == BLOCKS - 1:
                    dve.wait_ge(s_rows, 2 * (BLOCKS - HELD))
                    dve.wait_ge(s_share, BLOCKS - HELD - 1)
                    nc.vector.tensor_tensor(rows[:, W:2 * W], rows[:, W:2 * W], kout[:, :], ALU.add)\
                      .then_inc(s_share, 1)
            for part_of in LAYER0:
                part_of(0, 0)
            dve.wait_ge(s_zero, N // HALF - 1)

            def one_pass(order, q0, m, s):
                for q, item in enumerate(order):
                    if q in CHAIN_AT:
                        LAYER0[CHAIN_AT.index(q)](m, s + 1)
                    between = None
                    if q == L - 1 and item == BODY[-1]:
                        between = lambda: layer0_mass_low(m, s + 1)
                    last = order[q - 2] if q >= 2 else None
                    add = last is not None and last[0] == "A"
                    if add and item is not None and item[0] == "A":
                        between = lambda: add_part(m, s, last[1], q0 + q - 2)
                    if item is not None:
                        split(q0 + q, m, item, between)
                    if add and not (item is not None and item[0] == "A"):
                        add_part(m, s, last[1], q0 + q - 2)
                for q in range(len(order) - 2, len(order)):
                    if order[q][0] == "A":
                        add_part(m, s, order[q][1], q0 + q)
                if order is LAST_BODY:
                    layer0_mass_low(m, s + 1)

            with dve.Fori(0, PASSES) as m:
                one_pass(BODY, HEAD, m, 0)
            one_pass(LAST_BODY, LAST, 0, PASSES)

            for e in range(2 * BLOCKS):
                if 0 <= e - 2 < BLOCKS:
                    split(TAIL + e, 0, ITEMS[TAIL + e], lambda: add_part(0, BLOCKS - 1, e - 2, TAIL + e - 2))
                else:
                    split(TAIL + e, 0, ITEMS[TAIL + e])
                if 0 <= e - Z_SPLIT < BLOCKS:
                    c = e - Z_SPLIT
                    dve.wait_ge(s_zhi, c + 1)
                    nc.vector.tensor_tensor(w_lo[:, c * W:(c + 1) * W], turned[:, c % 4, :],
                                            w_hi[:, c * W:(c + 1) * W].bitcast(F32), ALU.subtract).then_inc(s_zlo, 1)

            def finish(g, m, j, b):
                base = BLOCKS * CHAIN + m * (2 * CHAIN_END) + j * CHAIN_END
                if g == SUM_AT:
                    chain[0] = 0
                    dve.wait_ge(s_rt, m * 2 + j + 1)
                    dve.wait_ge(s_x1in[b], m * 16 + 16 * (j // 2 + 1))
                    link(nc.vector.tensor_tensor(x1_in[:, b, :], turned[:, 2 + b, :], x1_in[:, b, :], ALU.add), base)
                    statistics(x1_in[:, b, :], base)
                if g == ROOT_AT:
                    reciprocal_root(m * 2, BLOCKS + j, base)
                    for k in range(SUB):
                        ins = centre(fin[:, b, :], x1_in[:, b, :], k)
                    ins.then_inc(s_fin, 1)
                    assert chain[0] == CHAIN_END

            def final(q0, m, j, b):
                for g in range(BLOCKS):
                    split(q0 + g, m, ("Z", g))
                    finish(g, m, j, b)

            with dve.Fori(0, (BLOCKS - 2) // 2) as m:
                final(FINAL + BLOCKS, m, 0, 0)
                final(FINAL + 2 * BLOCKS, m, 1, 1)
            final(FINAL + (BLOCKS - 1) * BLOCKS, 0, BLOCKS - 2, 0)
            for g in range(BLOCKS):
                finish(g, 0, BLOCKS - 1, 1)

        @block.tensor
        def _(pe):
            def multiply(dst, left_hi, left_lo, first_tile, q, m, start, stop, ahead=None, between=None):
                for h in range(2):
                    at = (2 * q + h) % SPLIT
                    pe.wait_ge(s_hi, halves(q, m, h))
                    for k in range(2):
                        cols = slice((first_tile + 2 * h + k) * P, (first_tile + 2 * h + k + 1) * P)
                        moving = hi[:, at, k * W:(k + 1) * W]
                        nc.tensor.matmul(dst, left_hi[:, cols], moving, start=(start and h == 0 and k == 0), stop=False)
                        nc.tensor.matmul(dst, left_lo[:, cols], moving, start=False, stop=False)
                    wait_low(pe, q, m, h)
                    for k in range(2):
                        cols = slice((first_tile + 2 * h + k) * P, (first_tile + 2 * h + k + 1) * P)
                        ins = nc.tensor.matmul(dst, left_hi[:, cols], lo[:, at, k * W:(k + 1) * W],
                                               start=False, stop=(stop and h == 1 and k == 1))
                    ins.then_inc(s_half, step_for(q, h))
                    if ahead is not None and is_turned(ahead):
                        turn_half(ahead, q + 2, m, h)
                    if between is not None and h == 0:
                        between()

            def turn_half(item, q, m, h):
                landed(pe, q, m)
                if item[1] > BLOCKS - HELD:
                    wait_low(pe, q - 1, m, h)
                for k in range(2):
                    for b in range(SUB):
                        at = b * W + (2 * h + k) * P
                        turn = nc.tensor.transpose(turned[:, 2 * h + k, b * P:(b + 1) * P],
                                                   raw[:, q % RAW, at:at + P], ident[:, :])
                turn.then_inc(s_turn, 1)

            def first_product(t, q, m, s, bank, ahead=None):
                if t == 0 and not (isinstance(m, int) and m + s < 2):
                    pe.wait_ge(s_aggc, m + s)
                multiply(bank, w_hi, w_lo, SUB * ((t + HELD) % BLOCKS), q, m, t == 0, False, ahead)
                if t == BLOCKS - 1:
                    pe.wait_ge(s_diag, m * SUB + SUB * (s + 1))
                    for k in range(SUB):
                        cols = slice(k * P, (k + 1) * P)
                        ins = nc.tensor.matmul(bank[:, cols], xi[:, cols], work[:, cols],
                                               start=False, stop=(k == SUB - 1))
                    ins.then_inc(s_agg, 1)
                    degree_product(m, s)

            def degree_product(m, s):
                pe.wait_ge(s_rows, m * (2 * (BLOCKS - HELD)) + 2 * (BLOCKS - HELD) * (s + 1))
                if isinstance(m, int) and m + s == 0:
                    pe.wait_ge(s_share, BLOCKS - HELD)
                for k in range(SUB):
                    for a in range(2):
                        ins = nc.tensor.matmul(turned[:, 3, k:k + 1], rows[:, a * W + k * P:a * W + (k + 1) * P],
                                               ones[:, :], start=(a == 0), stop=(a == 1))
                ins.then_inc(s_deg, 1)

            def feature_product(m, s):
                pe.wait_ge(s_aggc, m + s + 1)
                for k in range(SUB):
                    cols = slice(k * P, (k + 1) * P)
                    ins = nc.tensor.matmul(kout[:, k * F:(k + 1) * F], work[:, cols], k_sb[:, :], start=True, stop=True)
                ins.then_inc(s_kout, 1)

            def second_product(c, q, m, s, ahead=None, between=None):
                if c == 0:
                    pe.wait_ge(s_y, m + s + 1)
                if c >= 1:
                    pe.wait_ge(s_added, m * BLOCKS + s * BLOCKS + c)
                multiply(part[:, c % 2, :], y_hi, y_lo, 0, q, m, True, True, ahead, between)

            pe.wait_ge(s_const, 16 * CONSTS)
            pe.wait_ge(s_ones, 1)
            pe.wait_ge(s_ident, 2)
            for n in range(HEAD):
                if ITEMS[n] is None:
                    continue
                t = ITEMS[n][1]
                if n < BLOCKS:
                    pe.wait_ge(s_wlo, max(u + HELD for u in range(n + 1) if u < BLOCKS - HELD) // 4 + 1)
                    first_product(t, n, 0, 0, part[:, 0, :], ITEMS[n + 2] if n + 2 < BLOCKS else None)
                else:
                    first_product(t, n, 0, 1, acc[:, :])
                    if t == 0:
                        feature_product(0, 0)

            def one_pass(order, q0, m, s):
                for q, item in enumerate(order):
                    kind, t = item or (None, None)
                    ahead = order[q + 2] if q + 2 < len(order) else None
                    if item is None:
                        pass
                    elif kind == "A":
                        between = (lambda: feature_product(m, s + 1)) if q == FEATURES_AT else None
                        second_product(t, q0 + q, m, s, ahead, between)
                    elif t >= LEAD:
                        first_product(t, q0 + q, m, s + 1, acc[:, :], ahead)
                    else:
                        first_product(t, q0 + q, m, s + 2, acc[:, :], ahead)

            with pe.Fori(0, PASSES) as m:
                one_pass(BODY, HEAD, m, 0)
            one_pass(LAST_BODY, LAST, 0, PASSES)

            for e in range(2 * BLOCKS):
                if e < BLOCKS:
                    second_product(e, TAIL + e, 0, BLOCKS - 1)
                else:
                    pe.wait_ge(s_zlo, e - BLOCKS + 1)
                    multiply(acc[:, :], w_hi, w_lo, SUB * (e - BLOCKS), TAIL + e, 0,
                             e == BLOCKS, e == 2 * BLOCKS - 1)
                c = e - Z_TURN
                if 0 <= c < BLOCKS:
                    pe.wait_ge(s_coef, 2 * (c + 1))
                    if c >= 4:
                        pe.wait_ge(s_zlo, c - 3)
                    for k in range(SUB):
                        at = c * W + k * P
                        turn = nc.tensor.transpose(turned[:, c % 4, k * P:(k + 1) * P], spec[:, at:at + P], ident[:, :])
                    turn.then_inc(s_zt, 1)
            def finish(g, m, j, b):
                if g == TURN_AT:
                    pe.wait_ge(s_res, m * 2 + j + 1)
                    for k in range(SUB):
                        cols = slice(k * P, (k + 1) * P)
                        turn = nc.tensor.transpose(turned[:, 2 + b, cols], res_t[:, b, cols], ident[:, :])
                    turn.then_inc(s_rt, 1)

            def final(q0, m, j, b):
                for g in range(BLOCKS):
                    multiply(acc_end[1 - b][:, :], w_hi, w_lo, SUB * g, q0 + g, m, g == 0, g == BLOCKS - 1)
                    finish(g, m, j, b)

            with pe.Fori(0, (BLOCKS - 2) // 2) as m:
                final(FINAL + BLOCKS, m, 0, 0)
                final(FINAL + 2 * BLOCKS, m, 1, 1)
            final(FINAL + (BLOCKS - 1) * BLOCKS, 0, BLOCKS - 2, 0)
            finish(TURN_AT, 0, BLOCKS - 1, 1)


def kernel(**inputs):
    import numpy as np
    import concourse.bacc as bacc
    from concourse.bass_utils import run_bass_kernel_spmd

    adj = np.asarray(inputs["adj"])
    x = np.asarray(inputs["x"])
    beta_mass = np.stack([np.asarray(inputs["L0_gnn_beta"]), np.asarray(inputs["L1_gnn_mass"])])
    arrays = {
        "adj_t": adj.reshape(BLOCKS, W, BLOCKS, SUB, P).transpose(0, 2, 4, 3, 1).reshape(-1, P, CHUNK),
        "adj_n": adj.reshape(BLOCKS, SUB, P, BLOCKS, W).transpose(0, 3, 2, 1, 4).reshape(-1, P, CHUNK),
        "x_tiles": x.reshape(TILES, P, F).transpose(1, 0, 2).reshape(P, TILES * F),
        "x_blocks": x.reshape(BLOCKS, SUB, P, F).transpose(0, 2, 1, 3).reshape(BLOCKS, P, SUB * F),
        "beta_mass": beta_mass.reshape(2, BLOCKS, SUB, P).transpose(1, 3, 0, 2).reshape(BLOCKS, P, 2 * SUB),
        "gnn_kernel": np.asarray(inputs["L0_gnn_kernel"]),
        "bias": np.asarray(inputs["L0_gnn_bias"]),
        "evals0": np.asarray(inputs["L1_gnn_evals0"]),
        "evals1": np.asarray(inputs["L1_gnn_evals1"]),
        "times": np.asarray(inputs["L1_gnn_diffusion_time"]).T,
    }
    arrays = {name: np.ascontiguousarray(a) for name, a in arrays.items()}
    nc = bacc.Bacc("TRN2", target_bir_lowering=False, num_devices=1)
    args = [nc.dram_tensor(name, a.shape, F32, kind="ExternalInput").ap() for name, a in arrays.items()]
    args.append(nc.dram_tensor("x1_store", (BLOCKS, P, SUB * F), F32).ap())
    args.append(nc.dram_tensor("out", (N, F), F32, kind="ExternalOutput").ap())
    build(nc, *args)
    result = run_bass_kernel_spmd(nc, [arrays], core_ids=[0])
    return result.results[0]["out"]
```
